# Optimizing a Trainium2 kernel written in Bass

```python
import numpy as np
import jax
import jax.numpy as jnp

def _softmax(x, axis=-1):
    return jax.nn.softmax(x, axis=axis)

def _gelu(x):
    return jax.nn.gelu(x, approximate=True)

def _silu(x):
    return jax.nn.silu(x)

def _sigmoid(x):
    return jax.nn.sigmoid(x)

def _layernorm(x, axis=-1, eps=1e-05):
    m = jnp.mean(x, axis=axis, keepdims=True)
    v = jnp.var(x, axis=axis, keepdims=True)
    return (x - m) / jnp.sqrt(v + eps)

def _scatter_add(tgt, idx, src, axis=0):
    return tgt.at[idx].add(src)

def _segment_sum(src, seg, n):
    return jax.ops.segment_sum(src, seg, n)
kernel_name = 'mk_dlrm_tower_d1_rec_r8_f61194'

def setup_inputs(seed: int=0):
    np.random.seed(seed)
    _w = jnp.asarray

    def _rec_inputs():
        import jax
        import jax.numpy as jnp
        _tk = jax.random.key(seed)
        ids = jnp.stack([jax.random.randint(jax.random.fold_in(_tk, 200 + f), (512,), 0, v, jnp.int32) for f, v in enumerate([1250, 1250, 1250, 1250, 1000, 1250, 1000, 125000, 1000, 1250, 1250, 1000, 12500, 12500, 1000, 1000, 1000, 1000, 1000, 1000, 1250, 12500, 1250, 1000, 1000, 1000])], axis=1)
        tbl_0 = 0.05 * jax.random.normal(jax.random.fold_in(_tk, 500 + 0), (1250, 128), jnp.float32)
        tbl_1 = 0.05 * jax.random.normal(jax.random.fold_in(_tk, 500 + 1), (1250, 128), jnp.float32)
        tbl_2 = 0.05 * jax.random.normal(jax.random.fold_in(_tk, 500 + 2), (1250, 128), jnp.float32)
        tbl_3 = 0.05 * jax.random.normal(jax.random.fold_in(_tk, 500 + 3), (1250, 128), jnp.float32)
        tbl_4 = 0.05 * jax.random.normal(jax.random.fold_in(_tk, 500 + 4), (1000, 128), jnp.float32)
        tbl_5 = 0.05 * jax.random.normal(jax.random.fold_in(_tk, 500 + 5), (1250, 128), jnp.float32)
        tbl_6 = 0.05 * jax.random.normal(jax.random.fold_in(_tk, 500 + 6), (1000, 128), jnp.float32)
        tbl_7 = 0.05 * jax.random.normal(jax.random.fold_in(_tk, 500 + 7), (125000, 128), jnp.float32)
        tbl_8 = 0.05 * jax.random.normal(jax.random.fold_in(_tk, 500 + 8), (1000, 128), jnp.float32)
        tbl_9 = 0.05 * jax.random.normal(jax.random.fold_in(_tk, 500 + 9), (1250, 128), jnp.float32)
        tbl_10 = 0.05 * jax.random.normal(jax.random.fold_in(_tk, 500 + 10), (1250, 128), jnp.float32)
        tbl_11 = 0.05 * jax.random.normal(jax.random.fold_in(_tk, 500 + 11), (1000, 128), jnp.float32)
        tbl_12 = 0.05 * jax.random.normal(jax.random.fold_in(_tk, 500 + 12), (12500, 128), jnp.float32)
        tbl_13 = 0.05 * jax.random.normal(jax.random.fold_in(_tk, 500 + 13), (12500, 128), jnp.float32)
        tbl_14 = 0.05 * jax.random.normal(jax.random.fold_in(_tk, 500 + 14), (1000, 128), jnp.float32)
        tbl_15 = 0.05 * jax.random.normal(jax.random.fold_in(_tk, 500 + 15), (1000, 128), jnp.float32)
        tbl_16 = 0.05 * jax.random.normal(jax.random.fold_in(_tk, 500 + 16), (1000, 128), jnp.float32)
        tbl_17 = 0.05 * jax.random.normal(jax.random.fold_in(_tk, 500 + 17), (1000, 128), jnp.float32)
        tbl_18 = 0.05 * jax.random.normal(jax.random.fold_in(_tk, 500 + 18), (1000, 128), jnp.float32)
        tbl_19 = 0.05 * jax.random.normal(jax.random.fold_in(_tk, 500 + 19), (1000, 128), jnp.float32)
        tbl_20 = 0.05 * jax.random.normal(jax.random.fold_in(_tk, 500 + 20), (1250, 128), jnp.float32)
        tbl_21 = 0.05 * jax.random.normal(jax.random.fold_in(_tk, 500 + 21), (12500, 128), jnp.float32)
        tbl_22 = 0.05 * jax.random.normal(jax.random.fold_in(_tk, 500 + 22), (1250, 128), jnp.float32)
        tbl_23 = 0.05 * jax.random.normal(jax.random.fold_in(_tk, 500 + 23), (1000, 128), jnp.float32)
        tbl_24 = 0.05 * jax.random.normal(jax.random.fold_in(_tk, 500 + 24), (1000, 128), jnp.float32)
        tbl_25 = 0.05 * jax.random.normal(jax.random.fold_in(_tk, 500 + 25), (1000, 128), jnp.float32)
        _rk = jax.random.fold_in(_tk, 7)
        r_bottom_output = -0.000520686 + 1.00062 * jax.random.normal(jax.random.fold_in(_rk, 101), (512, 128), jnp.float32)
        W_top1 = 0.0456912 * jax.random.normal(jax.random.fold_in(_tk, 801), (479, 512), jnp.float32)
        W_top2 = 0.0441942 * jax.random.normal(jax.random.fold_in(_tk, 802), (512, 256), jnp.float32)
        W_top3 = 0.0625 * jax.random.normal(jax.random.fold_in(_tk, 803), (256, 1), jnp.float32)
        b_top1 = jnp.zeros((512,), jnp.float32)
        b_top2 = jnp.zeros((256,), jnp.float32)
        return (r_bottom_output, ids, tbl_0, tbl_1, tbl_2, tbl_3, tbl_4, tbl_5, tbl_6, tbl_7, tbl_8, tbl_9, tbl_10, tbl_11, tbl_12, tbl_13, tbl_14, tbl_15, tbl_16, tbl_17, tbl_18, tbl_19, tbl_20, tbl_21, tbl_22, tbl_23, tbl_24, tbl_25, W_top1, b_top1, W_top2, b_top2, W_top3)
    r_bottom_output, ids, tbl_0, tbl_1, tbl_2, tbl_3, tbl_4, tbl_5, tbl_6, tbl_7, tbl_8, tbl_9, tbl_10, tbl_11, tbl_12, tbl_13, tbl_14, tbl_15, tbl_16, tbl_17, tbl_18, tbl_19, tbl_20, tbl_21, tbl_22, tbl_23, tbl_24, tbl_25, W_top1, b_top1, W_top2, b_top2, W_top3 = _rec_inputs()

    def _L0_rec_setup():
        import jax, jax.numpy as jnp
        import numpy as np
        NUM_FEATURES = 27
        _TRIU_I, _TRIU_J = np.triu_indices(NUM_FEATURES, k=1)
        key = jax.random.key(seed)
        k1, k2 = jax.random.split(key)
        bottom_output = jax.random.normal(k1, (2048, 128), dtype=jnp.float32)
        embeddings = jax.random.normal(k2, (2048, 26, 128), dtype=jnp.float32)
        return {'bottom_output': bottom_output, 'embeddings': embeddings}
    _L0_rec_all = _L0_rec_setup()
    _L0_rec_in = {k: v for k, v in _L0_rec_all.items() if k in ()}
    del _L0_rec_all
    return {'r_bottom_output': r_bottom_output, 'ids': ids, 'tbl_0': tbl_0, 'tbl_1': tbl_1, 'tbl_2': tbl_2, 'tbl_3': tbl_3, 'tbl_4': tbl_4, 'tbl_5': tbl_5, 'tbl_6': tbl_6, 'tbl_7': tbl_7, 'tbl_8': tbl_8, 'tbl_9': tbl_9, 'tbl_10': tbl_10, 'tbl_11': tbl_11, 'tbl_12': tbl_12, 'tbl_13': tbl_13, 'tbl_14': tbl_14, 'tbl_15': tbl_15, 'tbl_16': tbl_16, 'tbl_17': tbl_17, 'tbl_18': tbl_18, 'tbl_19': tbl_19, 'tbl_20': tbl_20, 'tbl_21': tbl_21, 'tbl_22': tbl_22, 'tbl_23': tbl_23, 'tbl_24': tbl_24, 'tbl_25': tbl_25, 'W_top1': W_top1, 'b_top1': b_top1, 'W_top2': W_top2, 'b_top2': b_top2, 'W_top3': W_top3}

def reference(r_bottom_output, ids, tbl_0, tbl_1, tbl_2, tbl_3, tbl_4, tbl_5, tbl_6, tbl_7, tbl_8, tbl_9, tbl_10, tbl_11, tbl_12, tbl_13, tbl_14, tbl_15, tbl_16, tbl_17, tbl_18, tbl_19, tbl_20, tbl_21, tbl_22, tbl_23, tbl_24, tbl_25, W_top1, b_top1, W_top2, b_top2, W_top3):
    import jax
    import jax.numpy as jnp

    def _L0_rec_ref(bottom_output, embeddings):
        import jax, jax.numpy as jnp
        import numpy as np
        NUM_FEATURES = 27
        _TRIU_I, _TRIU_J = np.triu_indices(NUM_FEATURES, k=1)
        all_emb = jnp.concatenate([bottom_output[:, None, :], embeddings], axis=1)
        gram = jnp.einsum('bfd,bgd->bfg', all_emb, all_emb)
        return gram[:, _TRIU_I, _TRIU_J]
    e = jnp.stack([tbl_0[ids[:, 0]], tbl_1[ids[:, 1]], tbl_2[ids[:, 2]], tbl_3[ids[:, 3]], tbl_4[ids[:, 4]], tbl_5[ids[:, 5]], tbl_6[ids[:, 6]], tbl_7[ids[:, 7]], tbl_8[ids[:, 8]], tbl_9[ids[:, 9]], tbl_10[ids[:, 10]], tbl_11[ids[:, 11]], tbl_12[ids[:, 12]], tbl_13[ids[:, 13]], tbl_14[ids[:, 14]], tbl_15[ids[:, 15]], tbl_16[ids[:, 16]], tbl_17[ids[:, 17]], tbl_18[ids[:, 18]], tbl_19[ids[:, 19]], tbl_20[ids[:, 20]], tbl_21[ids[:, 21]], tbl_22[ids[:, 22]], tbl_23[ids[:, 23]], tbl_24[ids[:, 24]], tbl_25[ids[:, 25]]], axis=1)
    z = _L0_rec_ref(r_bottom_output, e)
    z = z.reshape(z.shape[0], -1)
    h = jnp.concatenate([z, r_bottom_output], axis=1)
    h = jnp.maximum(h @ W_top1 + b_top1, 0.0)
    h = jnp.maximum(h @ W_top2 + b_top2, 0.0)
    y = h @ W_top3
    return y

_drawn_inputs = setup_inputs


def setup_inputs(seed=0):
    import zlib

    import numpy as np

    out = dict(_drawn_inputs(seed))
    spreads = {'b_top1': (0.0, 0.1), 'b_top2': (0.0, 0.1)}
    factors = {}
    for name, (base, spread) in spreads.items():
        noise = np.random.default_rng([zlib.crc32(name.encode()), seed]).standard_normal(out[name].shape)
        drawn = base * np.exp(spread * noise) if base else spread * noise
        out[name] = jnp.asarray(drawn.astype(out[name].dtype))
    for name, factor in factors.items():
        out[name] = (out[name] * factor).astype(out[name].dtype)
    return out
```

```python
from contextlib import ExitStack

import concourse.bass as bass
from concourse import mybir

P = 128
B = 512
D = 128
FIELDS = 26
FEATS = FIELDS + 1
TILES = B // P
QUAD = 32
QUADS = P // QUAD
ONEHOT = [4, 6, 8, 11, 14, 15, 16, 17, 18, 19]
GATHERED = [f for f in range(FIELDS) if f not in ONEHOT]
NH = len(ONEHOT)
SLOT0 = 1 + NH
FEATURE_OF_SLOT = [0] + [1 + f for f in ONEHOT + GATHERED]
ROWS = 1000
OH_P = 125
OH_J = ROWS // OH_P
WHOLE = OH_P // 16 * 16
DELTAS = FEATS // 2
PAIRS = FEATS * DELTAS
ZCH = 3
ZI = FEATS // ZCH
ZK = ZI * DELTAS
H1 = 512
H2 = 256
N1 = H1 // P
N2 = H2 // P
GROUP = 4
GROUPS = [list(range(g, min(g + GROUP, len(GATHERED)))) for g in range(0, len(GATHERED), GROUP)]
CHUNKS = 4
PER_BANK = 4
BLK = QUADS * FEATS
OH_SLOTS = OH_J
RAW_BUFS = 3

ALU = mybir.AluOpType
ACT = mybir.ActivationFunctionType
F32 = mybir.dt.float32
F32R = mybir.dt.float32r
I32 = mybir.dt.int32
U32 = mybir.dt.uint32


def dlrm_tower(nc, x, out):
    with ExitStack() as ctx:
        def sb(name, shape, dt=F32):
            return ctx.enter_context(nc.sbuf_tensor(name, shape, dt))

        def sem(name):
            return ctx.enter_context(nc.semaphore(name))

        idx = sb("idx", [P, TILES, FIELDS], I32)
        ids_bc = sb("ids_bc", [P, NH, B], I32)
        emb = sb("emb", [P, TILES, len(GATHERED), D])
        bottom = sb("bottom", [P, TILES, D])
        emb_t = sb("emb_t", [D, B, QUAD])
        bottom_t = sb("bottom_t", [D, B])
        table = sb("table", [P, RAW_BUFS, OH_J, D])
        table_hi = sb("table_hi", [P, 2, OH_J, D], F32R)
        table_lo = sb("table_lo", [P, 2, OH_J, D], F32R)
        onehot = sb("onehot", [P, OH_SLOTS, B], F32R)
        row_no = sb("row_no", [P, OH_J])
        ident = sb("ident", [P, P])
        gram = sb("gram", [P, 2, FEATS, QUAD])
        z = sb("z", [P, FEATS + DELTAS, QUAD])
        pairs = sb("pairs", [P, ZCH, ZI, DELTAS])
        z_t = sb("z_t", [P, ZCH, P])
        w1z = sb("w1z", [P, ZCH, H1])
        w1b = sb("w1b", [P, H1])
        w2 = sb("w2", [P, N1, H2])
        w3 = sb("w3", [P, N2])
        b1 = sb("b1", [P, N1])
        b2 = sb("b2", [P, N2])
        h1 = sb("h1", [P, N1, P])
        h2 = sb("h2", [P, N2, P])
        y = sb("y", [1, B])

        turn = ctx.enter_context(nc.psum_tensor("turn", [P, 2, 512], F32))
        gps = ctx.enter_context(nc.psum_tensor("gps", [P, 2, 2, 512], F32))
        mps = ctx.enter_context(nc.psum_tensor("mps", [P, 2, 512], F32))

        idx_in = [sem(f"idx_in{i}") for i in range(2)]
        bottom_in = sem("bottom_in")
        ids_in = [sem(f"ids_in{n}") for n in range(NH)]
        table_in = [sem(f"table_in{i}") for i in range(RAW_BUFS)]
        w_in = sem("w_in")
        gathered = [[sem(f"gathered{t}_{g}") for g in range(len(GROUPS))] for t in range(TILES)]
        pad_zero = sem("pad_zero")
        ident_zero = sem("ident_zero")
        ident_ready = sem("ident_ready")
        row_no_ready = sem("row_no_ready")
        hi_ready = sem("hi_ready")
        lo_ready = sem("lo_ready")
        onehot_ready = sem("onehot_ready")
        onehot_used = sem("onehot_used")
        turned = sem("turned")
        turn_free = [sem(f"turn_free{i}") for i in range(2)]
        gram_done = sem("gram_done")
        gram_free_act = sem("gram_free_act")
        gram_free_dve = sem("gram_free_dve")
        z_ready = sem("z_ready")
        z_all_ready = sem("z_all_ready")
        pairs_act = sem("pairs_act")
        pairs_dve = sem("pairs_dve")
        z_turned = sem("z_turned")
        zt_ready = sem("zt_ready")
        l1_done = sem("l1_done")
        h1_act = sem("h1_act")
        h1_dve = sem("h1_dve")
        l2_done = sem("l2_done")
        h2_act = sem("h2_act")
        h2_dve = sem("h2_dve")
        l3_done = sem("l3_done")
        y_ready = sem("y_ready")
        out_done = sem("out_done")

        def turn_use(t, g):
            return 1 + NH + t * len(GROUPS) + g

        def zdiag(c):
            whole = z[:, :, :]
            return bass.AP(tensor=whole.tensor, offset=whole.offset + ZI * c * (QUAD + 1) + QUAD,
                           ap=[list(whole.ap[0]), [QUAD + 1, ZI], [QUAD, DELTAS]])

        def gram_block(t, c, s):
            rows = slice(QUAD * s, QUAD * (s + 1))
            dst = gram[rows, t % 2, :, c * 2 * PER_BANK:(c + 1) * 2 * PER_BANK]
            src = gps[rows, c % 2, :, 0:PER_BANK * BLK].rearrange("p b (r k) -> p b r k", k=BLK)
            return (dst.rearrange("p g (b r) -> p b r g", b=2), src[:, :, :, s * FEATS:(s + 1) * FEATS])

        steps = [("turn", 0), ("gram", 0)]
        for t in range(1, TILES - 1):
            steps += [("turn", t), ("pairs", t - 1), ("layer1", t - 1), ("gram", t), ("layer2", t - 1),
                      ("layer3", t - 1)]
        t = TILES - 1
        steps += [("pairs", t - 1), ("layer1", t - 1), ("layer2", t - 1), ("layer3", t - 1)]
        steps += [("turn", t), ("gram", t), ("pairs", t), ("layer1", t), ("layer2", t), ("layer3", t)]

        block = ctx.enter_context(nc.Block())

        @block.sync
        def _(sp):
            sp.dma_start(idx[:, 0, :], x["ids"][0:P, :]).then_inc(idx_in[0], 16)
            for n in range(NH):
                sp.dma_start(ids_bc[:, n, :], x["ids_by_slot"][n:n + 1, :].partition_broadcast(P)
                             ).then_inc(ids_in[n], 16)
                if n >= RAW_BUFS:
                    sp.wait_ge(lo_ready, n - RAW_BUFS + 1)
                src = x[f"tbl_{ONEHOT[n]}"].rearrange("(p j) d -> p j d", j=OH_J)
                sp.dma_start(table[0:WHOLE, n % RAW_BUFS, :, :], src[0:WHOLE]).then_inc(table_in[n % RAW_BUFS], 16)
                sp.dma_start(table[WHOLE:OH_P, n % RAW_BUFS, :, :], src[WHOLE:OH_P]
                             ).then_inc(table_in[n % RAW_BUFS], 16)
            sp.wait_ge(y_ready, TILES)
            sp.dma_start(out.rearrange("b o -> o b"), y[:, :]).then_inc(out_done, 16)
            sp.wait_ge(out_done, 16)

        @block.gpsimd
        def _(pool):
            nc.gpsimd.memset(ident[:, :], 0.0).then_inc(ident_zero, 1)
            nc.gpsimd.iota(row_no[:, :], [[1, OH_J]], base=0, channel_multiplier=OH_J,
                           allow_small_or_imprecise_dtypes=True).then_inc(row_no_ready, 1)
            pool.wait_ge(ident_zero, 1)
            nc.gpsimd.affine_select(out=ident[:, :], in_=ident[:, :], compare_op=ALU.not_equal, fill=1.0, base=0,
                                    pattern=[[-1, P]], channel_multiplier=1).then_inc(ident_ready, 1)
            for t in range(TILES):
                if t < 2:
                    pool.wait_ge(idx_in[t], 16)
                for g, members in enumerate(GROUPS):
                    for m in members:
                        f = GATHERED[m]
                        nc.gpsimd.indirect_dma_start(
                            emb[:, t, m, :], None, x[f"tbl_{f}"],
                            bass.IndirectOffsetOnAxis(ap=idx[:, t, f:f + 1].bitcast(U32), axis=0),
                        ).then_inc(gathered[t][g], 16)

        @block.scalar
        def _(act):
            act.dma_start(bottom[:, :, :], x["r_bottom_output"].rearrange("(t p) d -> p t d", p=P)
                          ).then_inc(bottom_in, 16)
            act.dma_start(idx[:, 1:TILES, :], x["ids"][P:B, :].rearrange("(t p) f -> p t f", p=P)
                          ).then_inc(idx_in[1], 16)
            act.dma_start(w1z[0:ZK, :, :], x["W1_pairs"].rearrange("(c k) n -> k c n", k=ZK)).then_inc(w_in, 16)
            act.dma_start(w1b[:, :], x["W1_bottom"]).then_inc(w_in, 16)
            act.dma_start(w2[:, :, :], x["W_top2"].rearrange("(c k) n -> k c n", k=P)).then_inc(w_in, 16)
            act.dma_start(w3[:, :], x["W3_cols"]).then_inc(w_in, 16)
            act.dma_start(b1[:, :], x["b1_cols"]).then_inc(w_in, 16)
            act.dma_start(b2[:, :], x["b2_cols"]).then_inc(w_in, 16)

            def split_hi(n):
                act.wait_ge(table_in[n % RAW_BUFS], 32 * (n // RAW_BUFS + 1))
                if n >= 2:
                    act.wait_ge(onehot_used, (n - 1) * OH_J)
                nc.scalar.copy(table_hi[0:OH_P, n % 2, :, :], table[0:OH_P, n % RAW_BUFS, :, :]
                               ).then_inc(hi_ready, 1)

            def product_out(n):
                act.wait_ge(onehot_used, (n + 1) * OH_J)
                nc.scalar.copy(emb_t[:, :, 1 + n], turn[:, (1 + n) % 2, :]).then_inc(turn_free[(1 + n) % 2], 1)

            act.wait_ge(turned, 1)
            for t in range(TILES):
                nc.scalar.copy(bottom_t[:, t * P:(t + 1) * P].rearrange("d (s r) -> d r s", s=QUADS),
                               turn[:, 0, t * P:(t + 1) * P].rearrange("d (r s) -> d r s", s=QUADS))
            nc.scalar.copy(emb_t[:, :, 0], turn[:, 0, :]).then_inc(turn_free[0], 1)
            split_hi(0)
            split_hi(1)
            for n in range(NH):
                product_out(n)
                if n + 2 < NH:
                    split_hi(n + 2)
            act.wait_ge(w_in, 96)
            for step, t in steps:
                if step == "turn":
                    for g, members in enumerate(GROUPS):
                        u = turn_use(t, g)
                        if u % 2 == 0:
                            act.wait_ge(turned, u - NH + 1)
                            m0 = SLOT0 + members[0]
                            nc.scalar.copy(emb_t[:, t * P:(t + 1) * P, m0:m0 + len(members)],
                                           turn[:, 0, 0:len(members) * P].rearrange("d (m b) -> d b m", b=P)
                                           ).then_inc(turn_free[0], 1)
                elif step == "gram":
                    for c in range(CHUNKS):
                        act.wait_ge(gram_done, t * CHUNKS + c + 1)
                        if c == 0 and t >= 2:
                            act.wait_ge(z_ready, t - 1)
                        for s in (0, 1):
                            last = nc.scalar.copy(*gram_block(t, c, s))
                        last.then_inc(gram_free_act, 1)
                elif step == "pairs":
                    if t >= 1:
                        act.wait_ge(z_turned, t)
                    act.wait_ge(z_ready, t + 1)
                    nc.scalar.copy(pairs[:, 0, :, :], zdiag(0))
                    act.wait_ge(z_all_ready, t + 1)
                    nc.scalar.copy(pairs[:, 1, :, :], zdiag(1)).then_inc(pairs_act, 1)
                elif step == "layer1":
                    act.wait_ge(l1_done, 2 * t + 1)
                    for m in (0, 1):
                        last = nc.scalar.activation(h1[:, m, :], mps[:, 1, m * P:(m + 1) * P], ACT.Relu,
                                                    bias=b1[:, m:m + 1])
                    last.then_inc(h1_act, 1)
                elif step == "layer2":
                    act.wait_ge(l2_done, 2 * t + 1)
                    nc.scalar.activation(h2[:, 0, :], mps[:, 1, 0:P], ACT.Relu, bias=b2[:, 0:1]).then_inc(h2_act, 1)
                elif step == "layer3":
                    act.wait_ge(l3_done, t + 1)
                    nc.scalar.copy(y[:, t * P:(t + 1) * P].rearrange("o (r s) -> o s r", s=QUADS),
                                   mps[0:1, 1, 0:P].rearrange("o (s r) -> o s r", s=QUADS)).then_inc(y_ready, 1)

        @block.vector
        def _(dve):
            nc.vector.memset(emb_t[:, :, FEATS:QUAD], 0.0).then_inc(pad_zero, 1)

            def split_lo(n):
                dve.wait_ge(hi_ready, n + 1)
                if n >= 2:
                    dve.wait_ge(onehot_used, (n - 1) * OH_J)
                nc.vector.tensor_tensor(table_lo[0:OH_P, n % 2, :, :], table[0:OH_P, n % RAW_BUFS, :, :],
                                        table_hi[0:OH_P, n % 2, :, :].bitcast(F32), ALU.subtract
                                        ).then_inc(lo_ready, 1)

            def make_onehot(n):
                dve.wait_ge(ids_in[n], 16)
                for j in range(OH_J):
                    k = n * OH_J + j
                    if k >= OH_SLOTS:
                        dve.wait_ge(onehot_used, k - OH_SLOTS + 1)
                    nc.vector.tensor_scalar(onehot[0:OH_P, k % OH_SLOTS, :], ids_bc[0:OH_P, n, :],
                                            row_no[0:OH_P, j:j + 1], None, ALU.is_equal).then_inc(onehot_ready, 1)

            dve.wait_ge(row_no_ready, 1)
            make_onehot(0)
            split_lo(0)
            split_lo(1)
            for n in range(1, NH):
                make_onehot(n)
                if n + 1 < NH:
                    split_lo(n + 1)
            dve.wait_ge(w_in, 96)
            for step, t in steps:
                if step == "turn":
                    for g, members in enumerate(GROUPS):
                        u = turn_use(t, g)
                        if u % 2 == 1:
                            dve.wait_ge(turned, u - NH + 1)
                            m0 = SLOT0 + members[0]
                            nc.vector.tensor_copy(emb_t[:, t * P:(t + 1) * P, m0:m0 + len(members)],
                                                  turn[:, 1, 0:len(members) * P].rearrange("d (m b) -> d b m", b=P)
                                                  ).then_inc(turn_free[1], 1)
                elif step == "gram":
                    for c in range(CHUNKS):
                        dve.wait_ge(gram_done, t * CHUNKS + c + 1)
                        for s in (2, 3):
                            last = nc.vector.tensor_copy(*gram_block(t, c, s))
                        last.then_inc(gram_free_dve, 1)
                    dve.wait_ge(gram_free_act, (t + 1) * CHUNKS)
                    dve.wait_ge(gram_free_dve, (t + 1) * CHUNKS)
                    if t >= 1:
                        dve.wait_ge(pairs_act, t)
                        dve.wait_ge(pairs_dve, t)
                    nc.vector.transpose(z[:, 0:FEATS, :].rearrange("p g f -> p (g f)"),
                                        gram[:, t % 2, :, :].rearrange("p g r -> p (g r)")).then_inc(z_ready, 1)
                    nc.vector.transpose(z[:, FEATS:FEATS + DELTAS, :].rearrange("p g f -> p (g f)"),
                                        gram[:, t % 2, 0:DELTAS, :].rearrange("p g r -> p (g r)")
                                        ).then_inc(z_all_ready, 1)
                elif step == "pairs":
                    dve.wait_ge(z_all_ready, t + 1)
                    if t >= 1:
                        dve.wait_ge(z_turned, t)
                    nc.vector.tensor_copy(pairs[:, 2, :, :], zdiag(2)).then_inc(pairs_dve, 1)
                    dve.wait_ge(z_turned, t + 1)
                    nc.vector.tensor_copy(z_t[0:ZK, :, :].rearrange("k c b -> k (c b)"), mps[0:ZK, 0, 0:ZCH * P]
                                          ).then_inc(zt_ready, 1)
                elif step == "layer1":
                    dve.wait_ge(l1_done, 2 * t + 2)
                    for m in (2, 3):
                        last = nc.vector.tensor_scalar(h1[:, m, :], mps[:, 0, (m - 2) * P:(m - 1) * P],
                                                       b1[:, m:m + 1], 0.0, ALU.add, ALU.max)
                    last.then_inc(h1_dve, 1)
                elif step == "layer2":
                    dve.wait_ge(l2_done, 2 * t + 2)
                    nc.vector.tensor_scalar(h2[:, 1, :], mps[:, 0, 0:P], b2[:, 1:2], 0.0, ALU.add, ALU.max
                                            ).then_inc(h2_dve, 1)

        @block.tensor
        def _(pe):
            pe.wait_ge(ident_ready, 1)
            pe.wait_ge(bottom_in, 16)
            for t in range(TILES):
                last = nc.tensor.transpose(turn[:, 0, t * P:(t + 1) * P], bottom[:, t, :], ident[:, :])
            last.then_inc(turned, 1)

            for n in range(NH):
                u = 1 + n
                if u >= 2:
                    pe.wait_ge(turn_free[u % 2], u // 2)
                pe.wait_ge(lo_ready, n + 1)
                for j in range(OH_J):
                    k = n * OH_J + j
                    pe.wait_ge(onehot_ready, k + 1)
                    nc.tensor.matmul(turn[:, u % 2, :], table_hi[0:OH_P, n % 2, j, :],
                                     onehot[0:OH_P, k % OH_SLOTS, :], start=(j == 0), stop=False)
                    last = nc.tensor.matmul(turn[:, u % 2, :], table_lo[0:OH_P, n % 2, j, :],
                                            onehot[0:OH_P, k % OH_SLOTS, :], start=False, stop=(j == OH_J - 1))
                    last.then_inc(onehot_used, 1)

            pe.wait_ge(pad_zero, 1)
            for step, t in steps:
                if step == "turn":
                    for g, members in enumerate(GROUPS):
                        u = turn_use(t, g)
                        pe.wait_ge(turn_free[u % 2], u // 2)
                        pe.wait_ge(gathered[t][g], 16 * len(members))
                        for i, m in enumerate(members):
                            last = nc.tensor.transpose(turn[:, u % 2, i * P:(i + 1) * P], emb[:, t, m, :], ident[:, :])
                        last.then_inc(turned, 1)
                elif step == "gram":
                    for bank in range(2):
                        uses = [u for u in range(turn_use(t, len(GROUPS))) if u % 2 == bank]
                        pe.wait_ge(turn_free[bank], len(uses))
                    for c in range(CHUNKS):
                        if t * CHUNKS + c >= 2:
                            pe.wait_ge(gram_free_act, t * CHUNKS + c - 1)
                            pe.wait_ge(gram_free_dve, t * CHUNKS + c - 1)
                        for i in range(2 * PER_BANK):
                            b0 = t * P + (c * 2 * PER_BANK + i) * QUADS
                            at = i % PER_BANK * BLK
                            last = nc.tensor.matmul(gps[:, c % 2, i // PER_BANK, at:at + BLK],
                                                    emb_t[:, b0:b0 + QUADS, :].rearrange("d s f -> d (s f)"),
                                                    emb_t[:, b0:b0 + QUADS, 0:FEATS], start=True, stop=True)
                        last.then_inc(gram_done, 1)
                elif step == "pairs":
                    pe.wait_ge(pairs_act, t + 1)
                    pe.wait_ge(pairs_dve, t + 1)
                    for c in range(ZCH):
                        last = nc.tensor.transpose(mps[0:ZK, 0, c * P:(c + 1) * P],
                                                   pairs[:, c, :, :].rearrange("p i d -> p (i d)"), ident[:, :])
                    last.then_inc(z_turned, 1)
                elif step == "layer1":
                    pe.wait_ge(w_in, 96)
                    if t >= 1:
                        pe.wait_ge(y_ready, t)
                    pe.wait_ge(zt_ready, t + 1)
                    for m in range(N1):
                        o = mps[:, 1 - m // 2, m % 2 * P:(m % 2 + 1) * P]
                        nc.tensor.matmul(o, w1b[:, m * P:(m + 1) * P], bottom_t[:, t * P:(t + 1) * P],
                                         start=True, stop=False)
                        for c in range(ZCH):
                            last = nc.tensor.matmul(o, w1z[0:ZK, c, m * P:(m + 1) * P], z_t[0:ZK, c, :],
                                                    start=False, stop=(c == ZCH - 1))
                        if m % 2 == 1:
                            last.then_inc(l1_done, 1)
                elif step == "layer2":
                    pe.wait_ge(h1_act, t + 1)
                    pe.wait_ge(h1_dve, t + 1)
                    for m in range(N2):
                        for c in range(N1):
                            last = nc.tensor.matmul(mps[:, 1 - m, 0:P], w2[:, c, m * P:(m + 1) * P], h1[:, c, :],
                                                    start=(c == 0), stop=(c == N1 - 1))
                        last.then_inc(l2_done, 1)
                elif step == "layer3":
                    pe.wait_ge(h2_act, t + 1)
                    pe.wait_ge(h2_dve, t + 1)
                    for m in range(N2):
                        last = nc.tensor.matmul(mps[0:1, 1, 0:P], w3[:, m:m + 1], h2[:, m, :],
                                                start=(m == 0), stop=(m == N2 - 1))
                    last.then_inc(l3_done, 1)


def pair_rows():
    rows = []
    for i in range(FEATS):
        for delta in range(1, DELTAS + 1):
            a, b = sorted((FEATURE_OF_SLOT[i], FEATURE_OF_SLOT[(i + delta) % FEATS]))
            rows.append(a * FEATS - a * (a + 1) // 2 + b - a - 1)
    return rows


def kernel(**inputs):
    import numpy as np
    import concourse.bacc as bacc
    from concourse.bass_utils import run_bass_kernel_spmd

    given = {name: np.asarray(a) for name, a in inputs.items()}
    w1 = given["W_top1"]
    sent = {name: given[name] for name in ["r_bottom_output", "ids", "W_top2"] + [f"tbl_{f}" for f in range(FIELDS)]}
    sent["ids_by_slot"] = given["ids"].T[ONEHOT]
    sent["W1_pairs"] = w1[pair_rows()]
    sent["W1_bottom"] = w1[PAIRS:]
    sent["b1_cols"] = given["b_top1"].reshape(N1, P).T
    sent["b2_cols"] = given["b_top2"].reshape(N2, P).T
    sent["W3_cols"] = given["W_top3"].reshape(N2, P).T

    nc = bacc.Bacc("TRN2", target_bir_lowering=False, num_devices=1)
    arrays, args = {}, {}
    for name, a in sent.items():
        a = np.ascontiguousarray(a)
        arrays[f"in_{name}_dram"] = a
        args[name] = nc.dram_tensor(f"in_{name}_dram", a.shape, mybir.dt.from_np(a.dtype), kind="ExternalInput").ap()
    out = nc.dram_tensor("out_0_dram", (B, 1), F32, kind="ExternalOutput").ap()
    dlrm_tower(nc, args, out)
    r = run_bass_kernel_spmd(nc, [arrays], core_ids=[0])
    return r.results[0]["out_0_dram"]
```

```python
from contextlib import ExitStack

import concourse.bass as bass
from concourse import mybir

P = 128
B = 512
D = 128
FIELDS = 26
FEATS = FIELDS + 1
TILES = B // P
QUAD = 32
QUADS = P // QUAD
ONEHOT = [4, 6, 8, 11, 14, 15, 16, 17]
GATHERED = [f for f in range(FIELDS) if f not in ONEHOT]
NH = len(ONEHOT)
NG = len(GATHERED)
LOOKED = 1 + NH
FEATURE_OF_SLOT = [0] + [1 + f for f in ONEHOT + GATHERED]
ROWS = 1000
OH_P = 125
OH_J = ROWS // OH_P
WHOLE = OH_P // 16 * 16
DELTAS = FEATS // 2
PAIRS = FEATS * DELTAS
ZCH = 3
ZI = FEATS // ZCH
ZK = ZI * DELTAS
H1 = 512
H2 = 256
N1 = H1 // P
N2 = H2 // P
GROUP_SIZES = [4, 4, 4, 4, 2]
GROUPS = [list(range(sum(GROUP_SIZES[:g]), sum(GROUP_SIZES[:g + 1]))) for g in range(len(GROUP_SIZES))]
CHUNKS = 4
PER_BANK = 4
BLK = QUADS * FEATS
RAW_BUFS = 3
SPLIT_BUFS = 3
EMB_BUFS = 3
ACT_QUADS = (0, 1)
DVE_QUADS = (2, 3)

ALU = mybir.AluOpType
ACT = mybir.ActivationFunctionType
F32 = mybir.dt.float32
F32R = mybir.dt.float32r
I32 = mybir.dt.int32
U32 = mybir.dt.uint32


def work_order():
    steps = [("ids", 0), ("onehot", 0), ("prepare", 0), ("ids", 1), ("prepare", 1)]
    between = {0: [("bottom", 0)], 1: [("turn", 0, 0)], 2: [("turn", 0, 1)], 3: [("turn", 0, 2)], 4: [("turn", 0, 3)],
               5: [("turn", 0, 4)], 6: [("turn", 1, 0)], 7: [("turn", 1, 1), ("pad", 0)]}
    for n in range(NH):
        steps.append(("product", n))
        if n + 1 < NH:
            steps.append(("onehot", n + 1))
        if n + 2 < NH:
            steps += [("ids", n + 2), ("prepare", n + 2)]
        steps.append(("product_out", n))
        steps += between.get(n, [])
    after = {(0, 0): [("turn", 1, 2)], (0, 1): [("turn", 1, 3)], (0, 2): [("turn", 1, 4)],
             (1, 0): [("base", 0), ("pairs", 0), ("turn", 2, 0)], (1, 1): [("layer1", 0), ("turn", 2, 1)],
             (1, 2): [("layer2", 0), ("turn", 2, 2)], (1, 3): [("layer3", 0)],
             (2, 0): [("base", 1), ("pairs", 1)], (2, 1): [("layer1", 1), ("turn", 3, 0)],
             (2, 2): [("layer2", 1), ("turn", 3, 1)], (2, 3): [("layer3", 1)]}
    for t in range(TILES):
        if t == 2:
            steps += [("turn", 2, 3), ("turn", 2, 4)]
        if t == 3:
            steps += [("base", 2), ("turn", 3, 2), ("pairs", 2), ("turn", 3, 3), ("turn", 3, 4)]
        for c in range(CHUNKS):
            steps += [("gram", t, c)] + after.get((t, c), [])
        steps.append(("relayout", t))
    return steps + [("layer1", 2), ("layer2", 2), ("layer3", 2), ("base", 3), ("pairs", 3), ("layer1", 3), ("layer2", 3), ("layer3", 3)]


def dlrm_tower(nc, x, out):
    with ExitStack() as ctx:
        def sb(name, shape, dt=F32):
            return ctx.enter_context(nc.sbuf_tensor(name, shape, dt))

        def sem(name):
            return ctx.enter_context(nc.semaphore(name))

        idx = sb("idx", [P, TILES, FIELDS], I32)
        ids_bc = sb("ids_bc", [P, 2, B], I32)
        ids_rel = sb("ids_rel", [P, 2, B])
        emb = sb("emb", [P, EMB_BUFS, NG, D])
        bottom = sb("bottom", [P, TILES, D])
        bottom_t = sb("bottom_t", [D, B])
        feat = sb("feat", [D, B, QUAD])
        table = sb("table", [P, RAW_BUFS, OH_J * D])
        table_hi = sb("table_hi", [P, SPLIT_BUFS, OH_J * D], F32R)
        table_lo = sb("table_lo", [P, SPLIT_BUFS, OH_J * D], F32R)
        onehot = sb("onehot", [P, OH_J, B], F32R)
        minus_row = sb("minus_row", [P, 1])
        ident = sb("ident", [P, P])
        gram = sb("gram", [P, 2, FEATS, QUAD])
        z = sb("z", [P, FEATS + DELTAS, QUAD])
        pairs = sb("pairs", [P, ZCH, ZI, DELTAS])
        z_t = sb("z_t", [P, ZCH * P])
        w1 = sb("w1", [P, ZCH + 1, H1])
        w2 = sb("w2", [P, N1, H2])
        w3 = sb("w3", [P, N2])
        b1 = sb("b1", [P, N1])
        b2 = sb("b2", [P, N2])
        h1 = sb("h1", [P, N1, P])
        h2 = sb("h2", [P, N2, P])
        y = sb("y", [1, B])

        turn = ctx.enter_context(nc.psum_tensor("turn", [P, 2, 512], F32))
        gps = ctx.enter_context(nc.psum_tensor("gps", [P, 2, 2, 512], F32))
        mps = ctx.enter_context(nc.psum_tensor("mps", [P, 2, 512], F32))

        idx_in = [sem(f"idx_in{i}") for i in range(2)]
        bottom_in = sem("bottom_in")
        ids_in = [sem(f"ids_in{i}") for i in range(2)]
        table_in = [sem(f"table_in{i}") for i in range(RAW_BUFS)]
        w_in = sem("w_in")
        gathered = [[sem(f"gathered{t}_{g}") for g in range(len(GROUPS))] for t in range(TILES)]
        minus_row_ready = sem("minus_row_ready")
        ident_zero = sem("ident_zero")
        ident_ready = sem("ident_ready")
        pad_zero = sem("pad_zero")
        bottom_turned = sem("bottom_turned")
        ids_ready = sem("ids_ready")
        hi_ready = sem("hi_ready")
        lo_ready = sem("lo_ready")
        onehot_ready = sem("onehot_ready")
        onehot_used = sem("onehot_used")
        product_done = sem("product_done")
        product_out = sem("product_out")
        turned = sem("turned")
        turn_free = [sem(f"turn_free{i}") for i in range(2)]
        feat_written = sem("feat_written")
        gram_done = sem("gram_done")
        gram_free_act = sem("gram_free_act")
        gram_free_dve = sem("gram_free_dve")
        z_ready = sem("z_ready")
        z_all_ready = sem("z_all_ready")
        pairs_act = sem("pairs_act")
        pairs_dve = sem("pairs_dve")
        z_turned = sem("z_turned")
        zt_ready = sem("zt_ready")
        l1_done = sem("l1_done")
        h1_act = sem("h1_act")
        h1_dve = sem("h1_dve")
        l2_done = sem("l2_done")
        h2_act = sem("h2_act")
        l3_done = sem("l3_done")
        y_ready = sem("y_ready")
        out_done = sem("out_done")

        steps = work_order()
        turn_use = {step: u for u, step in enumerate(s for s in steps if s[0] in ("bottom", "turn", "pairs", "layer2"))}
        turn_count = {step: n + 1 for n, step in enumerate(s for s in steps if s[0] == "turn")}

        def groups_until(t):
            return max(n for step, n in turn_count.items() if step[1] == t)

        def turn_bank(step):
            return turn_use[step] % 2

        def gram_block(t, c, s):
            rows = slice(QUAD * s, QUAD * (s + 1))
            dst = gram[rows, t % 2, :, c * 2 * PER_BANK:(c + 1) * 2 * PER_BANK]
            src = gps[rows, c % 2, :, 0:PER_BANK * BLK].rearrange("p b (r k) -> p b r k", k=BLK)
            return (dst.rearrange("p g (b r) -> p b r g", b=2), src[:, :, :, s * FEATS:(s + 1) * FEATS])

        def zdiag(c):
            whole = z[:, :, :]
            return bass.AP(tensor=whole.tensor, offset=whole.offset + ZI * c * (QUAD + 1) + QUAD,
                           ap=[list(whole.ap[0]), [QUAD + 1, ZI], [QUAD, DELTAS]])

        block = ctx.enter_context(nc.Block())

        @block.sync
        def _(sp):
            def load_ids(n):
                if n >= 2:
                    sp.wait_ge(ids_ready, n - 1)
                sp.dma_start(ids_bc[:, n % 2, :], x["ids_by_slot"][n:n + 1, :].partition_broadcast(P)
                             ).then_inc(ids_in[n % 2], 16)

            def buffer_free(n):
                if n >= RAW_BUFS:
                    sp.wait_ge(lo_ready, n - RAW_BUFS + 1)

            sp.dma_start(idx[:, 0, :], x["ids"][0:P, :]).then_inc(idx_in[0], 16)
            for n in range(NH):
                buffer_free(n)
                src = x[f"tbl_{ONEHOT[n]}"].rearrange("(p j) d -> p (j d)", j=OH_J)
                sp.dma_start(table[0:WHOLE, n % RAW_BUFS, :], src[0:WHOLE]).then_inc(table_in[n % RAW_BUFS], 16)
                sp.dma_start(table[WHOLE:OH_P, n % RAW_BUFS, :], src[WHOLE:OH_P]
                             ).then_inc(table_in[n % RAW_BUFS], 16)
                if n + 1 < NH:
                    load_ids(n + 1)
            sp.dma_start(w1[0:ZK, 0:ZCH, :], x["W1_pairs"].rearrange("(c k) n -> k c n", k=ZK)).then_inc(w_in, 16)
            sp.dma_start(w1[:, ZCH, :], x["W1_bottom"]).then_inc(w_in, 16)
            sp.dma_start(w2[:, :, :], x["W_top2"].rearrange("(c k) n -> k c n", k=P)).then_inc(w_in, 16)
            sp.dma_start(w3[:, :], x["W3_cols"]).then_inc(w_in, 16)
            sp.dma_start(b1[:, :], x["b1_cols"]).then_inc(w_in, 16)
            sp.dma_start(b2[:, :], x["b2_cols"]).then_inc(w_in, 16)
            sp.wait_ge(y_ready, TILES)
            sp.dma_start(out.rearrange("b o -> o b"), y[:, :]).then_inc(out_done, 16)
            sp.wait_ge(out_done, 16)

        @block.gpsimd
        def _(pool):
            nc.gpsimd.memset(ident[:, :], 0.0).then_inc(ident_zero, 1)
            nc.gpsimd.iota(minus_row[:, :], [[1, 1]], base=0, channel_multiplier=-OH_J,
                           allow_small_or_imprecise_dtypes=True).then_inc(minus_row_ready, 1)
            pool.wait_ge(ident_zero, 1)
            nc.gpsimd.affine_select(out=ident[:, :], in_=ident[:, :], compare_op=ALU.not_equal, fill=1.0, base=0,
                                    pattern=[[-1, P]], channel_multiplier=1).then_inc(ident_ready, 1)
            for t in range(TILES):
                if t < 2:
                    pool.wait_ge(idx_in[t], 16)
                for g, members in enumerate(GROUPS):
                    if t >= EMB_BUFS:
                        pool.wait_ge(turned, turn_count[("turn", t - EMB_BUFS, g)])
                    for m in members:
                        f = GATHERED[m]
                        nc.gpsimd.indirect_dma_start(
                            emb[:, t % EMB_BUFS, m, :], None, x[f"tbl_{f}"],
                            bass.IndirectOffsetOnAxis(ap=idx[:, t, f:f + 1].bitcast(U32), axis=0),
                        ).then_inc(gathered[t][g], 16)

        @block.scalar
        def _(act):
            act.dma_start(ids_bc[:, 0, :], x["ids_by_slot"][0:1, :].partition_broadcast(P)).then_inc(ids_in[0], 16)
            act.dma_start(bottom[:, :, :], x["r_bottom_output"].rearrange("(t p) d -> p t d", p=P)
                          ).then_inc(bottom_in, 16)
            act.dma_start(idx[:, 1:TILES, :], x["ids"][P:B, :].rearrange("(t p) f -> p t f", p=P)
                          ).then_inc(idx_in[1], 16)

            for step in steps:
                kind, t = step[:2]
                if kind == "bottom":
                    act.wait_ge(bottom_turned, 1)
                    nc.scalar.copy(bottom_t[:, :].rearrange("d (t s r) -> d t s r", s=QUADS, r=QUAD),
                                   turn[:, 0, :].rearrange("d (t r s) -> d t s r", s=QUADS, r=QUAD))
                    nc.scalar.copy(feat[:, :, 0], turn[:, 0, :]).then_inc(turn_free[0], 1)
                elif kind == "ids":
                    act.wait_ge(ids_in[t % 2], 16 * (t // 2 + 1))
                    if t == 0:
                        act.wait_ge(minus_row_ready, 1)
                    if t >= 2:
                        act.wait_ge(onehot_ready, (t - 1) * OH_J)
                    nc.scalar.activation(ids_rel[:, t % 2, :], ids_bc[:, t % 2, :], ACT.Identity,
                                         bias=minus_row[:, 0:1]).then_inc(ids_ready, 1)
                elif kind == "prepare":
                    act.wait_ge(table_in[t % RAW_BUFS], 32 * (t // RAW_BUFS + 1))
                    if t >= SPLIT_BUFS:
                        act.wait_ge(product_done, t - SPLIT_BUFS + 1)
                    nc.scalar.copy(table_hi[0:OH_P, t % SPLIT_BUFS, :], table[0:OH_P, t % RAW_BUFS, :]
                                   ).then_inc(hi_ready, 1)
                elif kind == "product_out":
                    act.wait_ge(product_done, t + 1)
                    nc.scalar.copy(feat[:, :, 1 + t], gps[:, t % 2, 0, :]).then_inc(product_out, 1)
                elif kind == "turn":
                    act.wait_ge(turned, turn_count[step])
                    members = GROUPS[step[2]]
                    m0 = LOOKED + members[0]
                    nc.scalar.copy(feat[:, t * P:(t + 1) * P, m0:m0 + len(members)],
                                   turn[:, turn_bank(step), 0:len(members) * P].rearrange("d (m b) -> d b m", b=P)
                                   ).then_inc(turn_free[turn_bank(step)], 1)
                elif kind == "gram":
                    c = step[2]
                    act.wait_ge(gram_done, t * CHUNKS + c + 1)
                    if c == 0 and t >= 2:
                        act.wait_ge(z_all_ready, t - 1)
                    for s in ACT_QUADS:
                        last = nc.scalar.copy(*gram_block(t, c, s))
                    last.then_inc(gram_free_act, 1)
                elif kind == "pairs":
                    if t >= 1:
                        act.wait_ge(z_turned, t)
                    act.wait_ge(z_ready, t + 1)
                    nc.scalar.copy(pairs[:, 0, :, :], zdiag(0))
                    act.wait_ge(z_all_ready, t + 1)
                    nc.scalar.copy(pairs[:, 1, :, :], zdiag(1)).then_inc(pairs_act, 1)
                elif kind == "layer1":
                    act.wait_ge(w_in, 96)
                    act.wait_ge(l1_done, 2 * t + 1)
                    for m in (0, 1):
                        last = nc.scalar.activation(h1[:, m, :], mps[:, 1, m * P:(m + 1) * P], ACT.Relu,
                                                    bias=b1[:, m:m + 1])
                    last.then_inc(h1_act, 1)
                elif kind == "layer2":
                    act.wait_ge(l2_done, 2 * t + 1)
                    nc.scalar.activation(h2[:, 0, :], mps[:, 1, 2 * P:3 * P], ACT.Relu, bias=b2[:, 0:1]).then_inc(h2_act, 1)
                elif kind == "layer3":
                    act.wait_ge(l3_done, t + 1)
                    nc.scalar.copy(y[:, t * P:(t + 1) * P].rearrange("o (r s) -> o s r", s=QUADS),
                                   mps[0:1, 0, 2 * P:3 * P].rearrange("o (s r) -> o s r", s=QUADS)).then_inc(y_ready, 1)

        @block.vector
        def _(dve):
            for step in steps:
                kind, t = step[:2]
                if kind == "pad":
                    nc.vector.memset(feat[:, :, FEATS:QUAD], 0.0).then_inc(pad_zero, 1)
                elif kind == "prepare":
                    dve.wait_ge(hi_ready, t + 1)
                    nc.vector.tensor_tensor(table_lo[0:OH_P, t % SPLIT_BUFS, :], table[0:OH_P, t % RAW_BUFS, :],
                                            table_hi[0:OH_P, t % SPLIT_BUFS, :].bitcast(F32), ALU.subtract
                                            ).then_inc(lo_ready, 1)
                elif kind == "onehot":
                    dve.wait_ge(ids_ready, t + 1)
                    for j in range(OH_J):
                        if t >= 1 and j < OH_J - 1:
                            dve.wait_ge(onehot_used, (t - 1) * (OH_J - 1) + j + 1)
                        elif t >= 1:
                            dve.wait_ge(product_done, t)
                        nc.vector.tensor_scalar(onehot[0:OH_P, j, :], ids_rel[0:OH_P, t % 2, :], float(j), None,
                                                ALU.is_equal).then_inc(onehot_ready, 1)
                elif kind == "gram":
                    c = step[2]
                    dve.wait_ge(gram_done, t * CHUNKS + c + 1)
                    for s in DVE_QUADS:
                        last = nc.vector.tensor_copy(*gram_block(t, c, s))
                    last.then_inc(gram_free_dve, 1)
                elif kind == "relayout":
                    dve.wait_ge(gram_free_act, (t + 1) * CHUNKS)
                    dve.wait_ge(gram_free_dve, (t + 1) * CHUNKS)
                    if t >= 1:
                        dve.wait_ge(pairs_act, t)
                        dve.wait_ge(pairs_dve, t)
                    nc.vector.transpose(z[:, 0:FEATS, :].rearrange("p g f -> p (g f)"),
                                        gram[:, t % 2, :, :].rearrange("p g r -> p (g r)")).then_inc(z_ready, 1)
                    nc.vector.transpose(z[:, FEATS:FEATS + DELTAS, :].rearrange("p g f -> p (g f)"),
                                        gram[:, t % 2, 0:DELTAS, :].rearrange("p g r -> p (g r)")
                                        ).then_inc(z_all_ready, 1)
                elif kind == "pairs":
                    dve.wait_ge(z_all_ready, t + 1)
                    if t >= 1:
                        dve.wait_ge(z_turned, t)
                    nc.vector.tensor_copy(pairs[:, 2, :, :], zdiag(2)).then_inc(pairs_dve, 1)
                    dve.wait_ge(z_turned, t + 1)
                    nc.vector.tensor_copy(z_t[0:ZK, :], turn[0:ZK, turn_bank(step), 0:ZCH * P]
                                          ).then_inc(turn_free[turn_bank(step)], 1)
                elif kind == "layer1":
                    dve.wait_ge(w_in, 96)
                    dve.wait_ge(l1_done, 2 * t + 2)
                    for m in (2, 3):
                        last = nc.vector.tensor_scalar(h1[:, m, :], mps[:, 0, (m - 2) * P:(m - 1) * P],
                                                       b1[:, m:m + 1], 0.0, ALU.add, ALU.max)
                    last.then_inc(h1_dve, 1)
                elif kind == "layer2":
                    dve.wait_ge(l2_done, 2 * t + 2)
                    nc.vector.tensor_scalar(h2[:, 1, :], turn[:, turn_bank(step), 0:P], b2[:, 1:2], 0.0, ALU.add,
                                            ALU.max).then_inc(turn_free[turn_bank(step)], 1)

        @block.tensor
        def _(pe):
            def turn_bank_free(step):
                u = turn_use[step]
                if u >= 2:
                    pe.wait_ge(turn_free[u % 2], u // 2)
                return u % 2

            def turn_result_read(step):
                pe.wait_ge(turn_free[turn_use[step] % 2], turn_use[step] // 2 + 1)

            for step in steps:
                kind, t = step[:2]
                if kind == "bottom":
                    pe.wait_ge(ident_ready, 1)
                    pe.wait_ge(bottom_in, 16)
                    for tile in range(TILES):
                        last = nc.tensor.transpose(turn[:, 0, tile * P:(tile + 1) * P], bottom[:, tile, :],
                                                   ident[:, :])
                    last.then_inc(bottom_turned, 1)
                elif kind == "product":
                    if t >= 2:
                        pe.wait_ge(product_out, t - 1)
                    pe.wait_ge(hi_ready, t + 1)
                    passes = [(j, part) for part in (0, 1) for j in range(OH_J)] if t == 0 else \
                        [(j, part) for j in range(OH_J) for part in (0, 1)]
                    for i, (j, part) in enumerate(passes):
                        if part == 0:
                            pe.wait_ge(onehot_ready, t * OH_J + j + 1)
                        if (i, part) in ((OH_J, 1), (1, 1)):
                            pe.wait_ge(lo_ready, t + 1)
                        mm = nc.tensor.matmul(gps[:, t % 2, 0, :],
                                              (table_hi, table_lo)[part][0:OH_P, t % SPLIT_BUFS, j * D:(j + 1) * D],
                                              onehot[0:OH_P, j, :], start=(i == 0), stop=(i == 2 * OH_J - 1))
                        if part == 1:
                            mm.then_inc(onehot_used if j < OH_J - 1 else product_done, 1)
                elif kind == "turn":
                    g = step[2]
                    bank = turn_bank_free(step)
                    pe.wait_ge(gathered[t][g], 16 * len(GROUPS[g]))
                    for i, m in enumerate(GROUPS[g]):
                        last = nc.tensor.transpose(turn[:, bank, i * P:(i + 1) * P], emb[:, t % EMB_BUFS, m, :],
                                                   ident[:, :])
                    last.then_inc(turned, 1)
                elif kind == "gram":
                    c = step[2]
                    if c == 0:
                        for step_before in list(turn_count)[groups_until(t) - 2:groups_until(t)]:
                            turn_result_read(step_before)
                    if t == 0 and c == 0:
                        pe.wait_ge(pad_zero, 1)
                        pe.wait_ge(product_out, NH)
                    if t * CHUNKS + c >= 2:
                        pe.wait_ge(gram_free_act, t * CHUNKS + c - 1)
                        pe.wait_ge(gram_free_dve, t * CHUNKS + c - 1)
                    for i in range(2 * PER_BANK):
                        b0 = t * P + (c * 2 * PER_BANK + i) * QUADS
                        at = i % PER_BANK * BLK
                        last = nc.tensor.matmul(gps[:, c % 2, i // PER_BANK, at:at + BLK],
                                                feat[:, b0:b0 + QUADS, :].rearrange("d s f -> d (s f)"),
                                                feat[:, b0:b0 + QUADS, 0:FEATS], start=True, stop=True)
                    last.then_inc(gram_done, 1)
                elif kind == "base":
                    if t == 0:
                        pe.wait_ge(w_in, 96)
                    else:
                        pe.wait_ge(y_ready, t)
                    for m in range(N1):
                        nc.tensor.matmul(mps[:, 1 - m // 2, m % 2 * P:(m % 2 + 1) * P], w1[:, ZCH, m * P:(m + 1) * P],
                                         bottom_t[:, t * P:(t + 1) * P], start=(m % 2 == 0), stop=False,
                                         skip_group_check=True)
                elif kind == "pairs":
                    bank = turn_bank_free(step)
                    pe.wait_ge(pairs_act, t + 1)
                    pe.wait_ge(pairs_dve, t + 1)
                    for c in range(ZCH):
                        last = nc.tensor.transpose(turn[0:ZK, bank, c * P:(c + 1) * P],
                                                   pairs[:, c, :, :].rearrange("p i d -> p (i d)"), ident[:, :])
                    last.then_inc(z_turned, 1)
                elif kind == "layer1":
                    turn_result_read(("pairs", t))
                    for m in range(N1):
                        for c in range(ZCH):
                            last = nc.tensor.matmul(mps[:, 1 - m // 2, m % 2 * P:(m % 2 + 1) * P],
                                                    w1[0:ZK, c, m * P:(m + 1) * P], z_t[0:ZK, c * P:(c + 1) * P],
                                                    start=False, stop=(c == ZCH - 1), skip_group_check=True)
                        if m % 2 == 1:
                            last.then_inc(l1_done, 1)
                elif kind == "layer2":
                    bank = turn_bank_free(step)
                    sums = [mps[:, 1, 2 * P:3 * P], turn[:, bank, 0:P]]
                    pe.wait_ge(h1_act, t + 1)
                    for c in range(N1):
                        if c == 2:
                            pe.wait_ge(h1_dve, t + 1)
                        for m in range(N2):
                            last = nc.tensor.matmul(sums[m], w2[:, c, m * P:(m + 1) * P], h1[:, c, :],
                                                    start=(c == 0), stop=(c == N1 - 1))
                            if c == N1 - 1:
                                last.then_inc(l2_done, 1)
                elif kind == "layer3":
                    pe.wait_ge(h2_act, t + 1)
                    turn_result_read(("layer2", t))
                    for m in range(N2):
                        last = nc.tensor.matmul(mps[0:1, 0, 2 * P:3 * P], w3[:, m:m + 1], h2[:, m, :],
                                                start=(m == 0), stop=(m == N2 - 1))
                    last.then_inc(l3_done, 1)


def pair_rows():
    rows = []
    for i in range(FEATS):
        for delta in range(1, DELTAS + 1):
            a, b = sorted((FEATURE_OF_SLOT[i], FEATURE_OF_SLOT[(i + delta) % FEATS]))
            rows.append(a * FEATS - a * (a + 1) // 2 + b - a - 1)
    return rows


def kernel(**inputs):
    import numpy as np
    import concourse.bacc as bacc
    from concourse.bass_utils import run_bass_kernel_spmd

    given = {name: np.asarray(a) for name, a in inputs.items()}
    w1 = given["W_top1"]
    sent = {name: given[name] for name in ["r_bottom_output", "ids", "W_top2"] + [f"tbl_{f}" for f in range(FIELDS)]}
    sent["ids_by_slot"] = given["ids"].T[ONEHOT]
    sent["W1_pairs"] = w1[pair_rows()]
    sent["W1_bottom"] = w1[PAIRS:]
    sent["b1_cols"] = given["b_top1"].reshape(N1, P).T
    sent["b2_cols"] = given["b_top2"].reshape(N2, P).T
    sent["W3_cols"] = given["W_top3"].reshape(N2, P).T

    nc = bacc.Bacc("TRN2", target_bir_lowering=False, num_devices=1)
    arrays, args = {}, {}
    for name, a in sent.items():
        a = np.ascontiguousarray(a)
        arrays[f"in_{name}_dram"] = a
        args[name] = nc.dram_tensor(f"in_{name}_dram", a.shape, mybir.dt.from_np(a.dtype), kind="ExternalInput").ap()
    out = nc.dram_tensor("out_0_dram", (B, 1), F32, kind="ExternalOutput").ap()
    dlrm_tower(nc, args, out)
    r = run_bass_kernel_spmd(nc, [arrays], core_ids=[0])
    return r.results[0]["out_0_dram"]
```

```python
from contextlib import ExitStack

import concourse.bass as bass
from concourse import mybir

P = 128
B = 512
D = 128
FIELDS = 26
FEATS = FIELDS + 1
TILES = B // P
QUAD = 32
QUADS = P // QUAD
ONEHOT = [4, 6, 8, 11, 14, 15, 16, 17, 18]
GATHERED = [f for f in range(FIELDS) if f not in ONEHOT]
NH = len(ONEHOT)
NG = len(GATHERED)
LOOKED = 1 + NH
FEATURE_OF_SLOT = [0] + [1 + f for f in ONEHOT + GATHERED]
ROWS = 1000
OH_P = 125
OH_J = ROWS // OH_P
WHOLE = OH_P // 16 * 16
HALF = OH_J * D // 2
DELTAS = FEATS // 2
PAIRS = FEATS * DELTAS
ZCH = 3
PAIR_CHUNKS = [[0], [1, 2]]
ZI = FEATS // ZCH
ZK = ZI * DELTAS
H1 = 512
H2 = 256
N1 = H1 // P
GROUP_SIZES = [4, 4, 4, 3, 2]
GROUPS = [list(range(sum(GROUP_SIZES[:g]), sum(GROUP_SIZES[:g + 1]))) for g in range(len(GROUP_SIZES))]
HALVES = 2
PER_BANK = QUAD // HALVES
WEIGHT_LOADS = 6
RAW_BUFS = 3
SPLIT_BUFS = 3
EMB_BUFS = 3
WARM_UP = 22

ALU = mybir.AluOpType
ACT = mybir.ActivationFunctionType
F32 = mybir.dt.float32
F32R = mybir.dt.float32r
I32 = mybir.dt.int32
U32 = mybir.dt.uint32


def work_order():
    steps = [("warm", 0), ("ids", 0), ("onehot", 0), ("prepare", 0), ("ids", 1), ("prepare", 1)]
    between = {0: [("bottom", 0), ("bottom_out", 0)], 1: [("turn", 0, 0)], 2: [("turn", 0, 1)], 3: [("turn", 0, 2)],
               4: [("turn", 0, 3)], 5: [("turn", 0, 4), ("turn", 1, 0)], 7: [("turn", 1, 1)],
               8: [("turn", 1, 2), ("turn", 1, 3)]}
    for n in range(NH):
        steps.append(("product", n))
        if n + 1 < NH:
            steps.append(("onehot", n + 1))
        if n + 2 < NH:
            steps += [("ids", n + 2), ("prepare", n + 2)]
        steps.append(("product_out", n))
        steps += between.get(n, [])
    return steps + [
        ("base", 0, 0), ("gram", 0, 0), ("turn", 1, 4), ("gram", 0, 1), ("relayout", 0), ("turn", 2, 0), ("pack", 0),
        ("gram", 1, 0), ("pairs", 0, 0), ("pairs", 0, 1), ("base", 0, 1), ("turn", 2, 1),
        ("gram", 1, 1), ("relayout", 1), ("pack", 1),
        ("layer1", 0, 0), ("layer1", 0, 1), ("turn", 2, 2), ("pairs", 1, 0), ("layer2", 0), ("sum", 0),
        ("pairs", 1, 1), ("turn", 2, 3), ("base", 1, 1), ("base", 1, 0), ("turn", 2, 4),
        ("layer1", 1, 0), ("layer1", 1, 1),
        ("gram", 2, 0), ("turn", 3, 0), ("gram", 2, 1), ("relayout", 2),
        ("layer2", 1), ("pack", 2), ("sum", 1), ("turn", 3, 1), ("base", 2, 1), ("pairs", 2, 0), ("turn", 3, 2),
        ("base", 2, 0), ("pairs", 2, 1), ("base", 3, 0),
        ("layer1", 2, 0), ("turn", 3, 3), ("layer1", 2, 1), ("turn", 3, 4), ("base", 3, 1),
        ("gram", 3, 0), ("gram", 3, 1), ("relayout", 3), ("pack", 3), ("layer2", 2),
        ("pairs", 3, 0), ("pairs", 3, 1), ("sum", 2),
        ("layer1", 3, 0), ("layer1", 3, 1), ("layer2", 3), ("sum", 3)]


def dlrm_tower(nc, x, out):
    with ExitStack() as ctx:
        def sb(name, shape, dt=F32):
            return ctx.enter_context(nc.sbuf_tensor(name, shape, dt))

        def sem(name):
            return ctx.enter_context(nc.semaphore(name))

        idx = sb("idx", [P, TILES, FIELDS], I32)
        ids_bc = sb("ids_bc", [P, 2, B], I32)
        ids_rel = sb("ids_rel", [P, 2, B])
        emb = sb("emb", [P, EMB_BUFS, NG, D])
        bottom = sb("bottom", [P, TILES, D])
        bottom_t = sb("bottom_t", [D, B])
        feat = sb("feat", [D, B, QUAD])
        table = sb("table", [P, RAW_BUFS, OH_J * D])
        table_hi = sb("table_hi", [P, SPLIT_BUFS, OH_J * D], F32R)
        table_lo = sb("table_lo", [P, SPLIT_BUFS, OH_J * D], F32R)
        onehot = sb("onehot", [P, OH_J, B], F32R)
        minus_row = sb("minus_row", [P, 1])
        row_copy = sb("row_copy", [P, 1])
        ident = sb("ident", [P, P])
        z = sb("z", [P, FEATS + DELTAS, QUAD])
        pairs = sb("pairs", [P, ZCH, ZI, DELTAS])
        z_t = sb("z_t", [P, ZCH * P])
        w1 = sb("w1", [P, ZCH + 1, H1])
        w2 = sb("w2", [P, N1, H2])
        w3 = sb("w3", [P, H2])
        b1 = sb("b1", [P, N1])
        b2 = sb("b2", [P, H2])
        h1 = sb("h1", [P, N1, P])
        ones = sb("ones", [1, P])
        h2 = sb("h2", [P, H2])
        weighted = sb("weighted", [P, H2])
        y = sb("y", [P, TILES])

        turn = ctx.enter_context(nc.psum_tensor("turn", [P, 2, 512], F32))
        gps = ctx.enter_context(nc.psum_tensor("gps", [P, 2, 2, 512], F32))
        mps = ctx.enter_context(nc.psum_tensor("mps", [P, 2, 512], F32))

        idx_in = [sem(f"idx_in{i}") for i in range(2)]
        bottom_in = sem("bottom_in")
        ids_in = [sem(f"ids_in{i}") for i in range(2)]
        table_in = [sem(f"table_in{i}") for i in range(RAW_BUFS)]
        w_in = sem("w_in")
        gathered = [[sem(f"gathered{t}_{g}") for g in range(len(GROUPS))] for t in range(TILES)]
        minus_row_ready = sem("minus_row_ready")
        ident_zero = sem("ident_zero")
        ident_ready = sem("ident_ready")
        pad_zero = sem("pad_zero")
        bottom_turned = sem("bottom_turned")
        ids_ready = sem("ids_ready")
        hi_first_half = sem("hi_first_half")
        hi_ready = sem("hi_ready")
        lo_first_half = sem("lo_first_half")
        lo_ready = sem("lo_ready")
        onehot_ready = sem("onehot_ready")
        onehot_used = sem("onehot_used")
        product_done = sem("product_done")
        product_out = sem("product_out")
        turned = sem("turned")
        turn_free = [sem(f"turn_free{i}") for i in range(2)]
        gram_done = sem("gram_done")
        z_ready = sem("z_ready")
        z_all_ready = sem("z_all_ready")
        pairs_act = sem("pairs_act")
        pairs_dve = sem("pairs_dve")
        z_turned = sem("z_turned")
        l1_done = sem("l1_done")
        h1_act = sem("h1_act")
        h1_dve = sem("h1_dve")
        l2_done = sem("l2_done")
        ones_ready = sem("ones_ready")
        h2_biased = sem("h2_biased")
        y_ready = sem("y_ready")
        out_done = sem("out_done")

        steps = work_order()
        turn_use = {step: u for u, step in enumerate(s for s in steps if s[0] in ("bottom", "turn", "pairs"))}
        turn_count = {step: n + 1 for n, step in enumerate(s for s in steps if s[0] == "turn")}

        def groups_until(t):
            return max(n for step, n in turn_count.items() if step[1] == t)

        def mlp_bank(t, bank):
            return gps[:, (t + 1) % 2, bank, :] if t == TILES - 1 else mps[:, bank, :]

        def turn_bank(step):
            return turn_use[step] % 2

        def gram_rows(t, rows):
            return gps[:, t % 2, :, :].rearrange("p h (r g) -> p g h r", g=QUAD)[:, 0:rows]

        def zdiag(c):
            whole = z[:, :, :]
            return bass.AP(tensor=whole.tensor, offset=whole.offset + ZI * c * (QUAD + 1) + QUAD,
                           ap=[list(whole.ap[0]), [QUAD + 1, ZI], [QUAD, DELTAS]])

        block = ctx.enter_context(nc.Block())

        @block.sync
        def _(sp):
            def load_ids(n):
                if n >= 2:
                    sp.wait_ge(ids_ready, n - 1)
                sp.dma_start(ids_bc[:, n % 2, :], x["ids_by_slot"][n:n + 1, :].partition_broadcast(P)
                             ).then_inc(ids_in[n % 2], 16)

            def buffer_free(n):
                if n >= RAW_BUFS:
                    sp.wait_ge(lo_ready, n - RAW_BUFS + 1)

            sp.dma_start(idx[:, 0, :], x["ids"][0:P, :]).then_inc(idx_in[0], 16)
            for n in range(NH):
                buffer_free(n)
                src = x[f"tbl_{ONEHOT[n]}"].rearrange("(p j) d -> p (j d)", j=OH_J)
                sp.dma_start(table[0:WHOLE, n % RAW_BUFS, :], src[0:WHOLE]).then_inc(table_in[n % RAW_BUFS], 16)
                sp.dma_start(table[WHOLE:OH_P, n % RAW_BUFS, :], src[WHOLE:OH_P]
                             ).then_inc(table_in[n % RAW_BUFS], 16)
                if n + 1 < NH:
                    load_ids(n + 1)
                if n == 1:
                    sp.dma_start(bottom[:, :, :], x["r_bottom_output"].rearrange("(t p) d -> p t d", p=P)
                                 ).then_inc(bottom_in, 16)
                    sp.dma_start(idx[:, 1:TILES, :], x["ids"][P:B, :].rearrange("(t p) f -> p t f", p=P)
                                 ).then_inc(idx_in[1], 16)
            sp.dma_start(w1[0:ZK, 0:ZCH, :], x["W1_pairs"].rearrange("(c k) n -> k c n", k=ZK)).then_inc(w_in, 16)
            sp.dma_start(w1[:, ZCH, :], x["W1_bottom"]).then_inc(w_in, 16)
            sp.dma_start(w2[:, :, :], x["W_top2"].rearrange("(c k) n -> k c n", k=P)).then_inc(w_in, 16)
            sp.dma_start(w3[:, :], x["W3_row"].partition_broadcast(P)).then_inc(w_in, 16)
            sp.dma_start(b1[:, :], x["b1_cols"]).then_inc(w_in, 16)
            sp.dma_start(b2[:, :], x["b2_row"].partition_broadcast(P)).then_inc(w_in, 16)
            for t in range(TILES):
                sp.wait_ge(y_ready, t + 1)
                sp.dma_start(out[t * P:(t + 1) * P, :].rearrange("(r s) o -> s r o", s=QUADS), y[:, t:t + 1],
                             allow_slow_non_contiguous=True).then_inc(out_done, 16)
            sp.wait_ge(out_done, 16 * TILES)

        @block.gpsimd
        def _(pool):
            nc.gpsimd.iota(minus_row[:, :], [[1, 1]], base=0, channel_multiplier=-OH_J,
                           allow_small_or_imprecise_dtypes=True).then_inc(minus_row_ready, 1)
            nc.gpsimd.memset(ident[:, :], 0.0).then_inc(ident_zero, 1)
            pool.wait_ge(ident_zero, 1)
            nc.gpsimd.affine_select(out=ident[:, :], in_=ident[:, :], compare_op=ALU.not_equal, fill=1.0, base=0,
                                    pattern=[[-1, P]], channel_multiplier=1).then_inc(ident_ready, 1)
            for t in range(TILES):
                if t < 2:
                    pool.wait_ge(idx_in[t], 16)
                for g, members in enumerate(GROUPS):
                    if t >= EMB_BUFS:
                        pool.wait_ge(turned, turn_count[("turn", t - EMB_BUFS, g)])
                    for m in members:
                        f = GATHERED[m]
                        nc.gpsimd.indirect_dma_start(
                            emb[:, t % EMB_BUFS, m, :], None, x[f"tbl_{f}"],
                            bass.IndirectOffsetOnAxis(ap=idx[:, t, f:f + 1].bitcast(U32), axis=0),
                        ).then_inc(gathered[t][g], 16)

        @block.scalar
        def _(act):
            act.dma_start(ids_bc[:, 0, :], x["ids_by_slot"][0:1, :].partition_broadcast(P)).then_inc(ids_in[0], 16)

            act.wait_ge(minus_row_ready, 1)
            nc.scalar.activation(row_copy[:, :], minus_row[:, :], ACT.Identity)

            for step in steps:
                kind, t = step[:2]
                if kind == "bottom_out":
                    act.wait_ge(bottom_turned, 1)
                    nc.scalar.copy(bottom_t[:, :].rearrange("d (t s r) -> d t s r", s=QUADS, r=QUAD),
                                   turn[:, 0, :].rearrange("d (t r s) -> d t s r", s=QUADS, r=QUAD))
                    nc.scalar.copy(feat[:, :, 0], turn[:, 0, :]).then_inc(turn_free[0], 1)
                elif kind == "ids":
                    act.wait_ge(ids_in[t % 2], 16 * (t // 2 + 1))
                    if t >= 2:
                        act.wait_ge(onehot_ready, (t - 1) * OH_J)
                    nc.scalar.activation(ids_rel[:, t % 2, :], ids_bc[:, t % 2, :], ACT.Identity,
                                         bias=minus_row[:, 0:1]).then_inc(ids_ready, 1)
                elif kind == "prepare":
                    act.wait_ge(table_in[t % RAW_BUFS], 32 * (t // RAW_BUFS + 1))
                    if t >= SPLIT_BUFS:
                        act.wait_ge(product_done, t - SPLIT_BUFS + 1)
                    if t == 0:
                        nc.scalar.copy(table_hi[0:OH_P, 0, 0:HALF], table[0:OH_P, 0, 0:HALF]).then_inc(hi_first_half, 1)
                    part = slice(HALF if t == 0 else 0, OH_J * D)
                    nc.scalar.copy(table_hi[0:OH_P, t % SPLIT_BUFS, part], table[0:OH_P, t % RAW_BUFS, part]
                                   ).then_inc(hi_ready, 1)
                elif kind == "product_out":
                    act.wait_ge(product_done, t + 1)
                    nc.scalar.copy(feat[:, :, 1 + t], gps[:, t % 2, 0, :]).then_inc(product_out, 1)
                elif kind == "turn":
                    act.wait_ge(turned, turn_count[step])
                    members = GROUPS[step[2]]
                    m0 = LOOKED + members[0]
                    nc.scalar.copy(feat[:, t * P:(t + 1) * P, m0:m0 + len(members)],
                                   turn[:, turn_bank(step), 0:len(members) * P].rearrange("d (m b) -> d b m", b=P)
                                   ).then_inc(turn_free[turn_bank(step)], 1)
                elif kind == "pack":
                    if t >= 1:
                        act.wait_ge(z_turned, 2 * t)
                    act.wait_ge(z_ready, t + 1)
                    nc.scalar.copy(pairs[:, 0, :, :], zdiag(0)).then_inc(pairs_act, 1)
                    act.wait_ge(z_all_ready, t + 1)
                    nc.scalar.copy(pairs[:, 1, :, :], zdiag(1)).then_inc(pairs_act, 1)
                elif kind == "layer1" and step[2] == 0:
                    act.wait_ge(w_in, 16 * WEIGHT_LOADS)
                    act.wait_ge(l1_done, 2 * t + 1)
                    for m in (0, 1):
                        last = nc.scalar.activation(h1[:, m, :], mlp_bank(t, 1)[:, m * P:(m + 1) * P], ACT.Relu,
                                                    bias=b1[:, m:m + 1])
                    last.then_inc(h1_act, 1)

        @block.vector
        def _(dve):
            nc.vector.memset(feat[:, :, FEATS:QUAD], 0.0).then_inc(pad_zero, 1)
            nc.vector.memset(ones[:, :], 1.0).then_inc(ones_ready, 1)
            for step in steps:
                kind, t = step[:2]
                if kind == "prepare":
                    dve.wait_ge(hi_ready, t + 1)
                    if t == 0:
                        dve.wait_ge(hi_first_half, 1)
                        nc.vector.tensor_tensor(table_lo[0:OH_P, 0, 0:HALF], table[0:OH_P, 0, 0:HALF],
                                                table_hi[0:OH_P, 0, 0:HALF].bitcast(F32), ALU.subtract
                                                ).then_inc(lo_first_half, 1)
                    part = slice(HALF if t == 0 else 0, OH_J * D)
                    nc.vector.tensor_tensor(table_lo[0:OH_P, t % SPLIT_BUFS, part], table[0:OH_P, t % RAW_BUFS, part],
                                            table_hi[0:OH_P, t % SPLIT_BUFS, part].bitcast(F32), ALU.subtract
                                            ).then_inc(lo_ready, 1)
                elif kind == "onehot":
                    dve.wait_ge(ids_ready, t + 1)
                    for j in range(OH_J):
                        if t >= 1 and j < OH_J - 1:
                            dve.wait_ge(onehot_used, (t - 1) * (OH_J - 1) + j + 1)
                        elif t >= 1:
                            dve.wait_ge(product_done, t)
                        nc.vector.tensor_scalar(onehot[0:OH_P, j, :], ids_rel[0:OH_P, t % 2, :], float(j), None,
                                                ALU.is_equal).then_inc(onehot_ready, 1)
                elif kind == "relayout":
                    dve.wait_ge(gram_done, t + 1)
                    if t >= 1:
                        dve.wait_ge(pairs_act, 2 * t)
                        dve.wait_ge(pairs_dve, t)
                    nc.vector.transpose(z[:, 0:FEATS, :].rearrange("p g (h r) -> p g h r", h=HALVES),
                                        gram_rows(t, FEATS)).then_inc(z_ready, 1)
                    nc.vector.transpose(z[:, FEATS:FEATS + DELTAS, :].rearrange("p g (h r) -> p g h r", h=HALVES),
                                        gram_rows(t, DELTAS)).then_inc(z_all_ready, 1)
                elif kind == "pack":
                    dve.wait_ge(z_all_ready, t + 1)
                    if t >= 1:
                        dve.wait_ge(z_turned, 2 * t)
                    nc.vector.tensor_copy(pairs[:, 2, :, :], zdiag(2)).then_inc(pairs_dve, 1)
                elif kind == "pairs":
                    if t >= 1:
                        dve.wait_ge(l1_done, 2 * t)
                    dve.wait_ge(z_turned, 2 * t + step[2] + 1)
                    chunks = PAIR_CHUNKS[step[2]]
                    nc.vector.tensor_copy(z_t[0:ZK, chunks[0] * P:(chunks[-1] + 1) * P],
                                          turn[0:ZK, turn_bank(step), 0:len(chunks) * P]
                                          ).then_inc(turn_free[turn_bank(step)], 1)
                elif kind == "layer1" and step[2] == 1:
                    dve.wait_ge(w_in, 16 * WEIGHT_LOADS)
                    dve.wait_ge(l1_done, 2 * t + 2)
                    for m in (2, 3):
                        nc.vector.tensor_scalar(h1[:, m, :], mlp_bank(t, 0)[:, (m - 2) * P:(m - 1) * P],
                                                b1[:, m:m + 1], 0.0, ALU.add, ALU.max).then_inc(h1_dve, 1)
                elif kind == "sum":
                    dve.wait_ge(l2_done, t + 1)
                    if t >= 1:
                        dve.wait_ge(y_ready, t)
                    sums = mlp_bank(t, 1)[:, 2 * P:2 * P + H2]
                    if t < TILES - 1:
                        nc.vector.tensor_tensor(h2[:, :], sums, b2[:, :], ALU.add).then_inc(h2_biased, 1)
                        dve.wait_ge(h2_biased, t + 1)
                    nc.vector.scalar_tensor_tensor(out=weighted[:, :], in0=h2[:, :] if t < TILES - 1 else sums,
                                                   scalar=0.0, in1=w3[:, :], op0=ALU.max, op1=ALU.mult,
                                                   accum_out=y[:, t:t + 1]).then_inc(y_ready, 1)

        @block.tensor
        def _(pe):
            def turn_bank_free(step):
                u = turn_use[step]
                if u >= 2:
                    pe.wait_ge(turn_free[u % 2], u // 2)
                return u % 2

            def turn_result_read(step):
                pe.wait_ge(turn_free[turn_use[step] % 2], turn_use[step] // 2 + 1)

            for step in steps:
                kind, t = step[:2]
                if kind == "warm":
                    pe.wait_ge(ident_ready, 1)
                    for _ in range(WARM_UP):
                        nc.tensor.transpose(turn[:, 1, 0:P], ident[:, :], ident[:, :])
                elif kind == "bottom":
                    pe.wait_ge(bottom_in, 16)
                    for tile in range(TILES):
                        last = nc.tensor.transpose(turn[:, 0, tile * P:(tile + 1) * P], bottom[:, tile, :],
                                                   ident[:, :])
                    last.then_inc(bottom_turned, 1)
                elif kind == "product":
                    if t >= 2:
                        pe.wait_ge(product_out, t - 1)
                    if t == 0:
                        pe.wait_ge(hi_first_half, 1)
                    else:
                        pe.wait_ge(hi_ready, t + 1)
                    passes = [(j, part) for part in (0, 1) for j in range(OH_J)] if t == 0 else \
                        [(j, part) for j in range(OH_J) for part in (0, 1)]
                    for i, (j, part) in enumerate(passes):
                        if t == 0 and (j, part) == (OH_J // 2, 0):
                            pe.wait_ge(hi_ready, 1)
                        if t == 0 and (j, part) == (0, 1):
                            pe.wait_ge(lo_first_half, 1)
                        if (j, part) == ((OH_J // 2, 1) if t == 0 else (0, 1)):
                            pe.wait_ge(lo_ready, t + 1)
                        if part == 0:
                            pe.wait_ge(onehot_ready, t * OH_J + j + 1)
                        mm = nc.tensor.matmul(gps[:, t % 2, 0, :],
                                              (table_hi, table_lo)[part][0:OH_P, t % SPLIT_BUFS, j * D:(j + 1) * D],
                                              onehot[0:OH_P, j, :], start=(i == 0), stop=(i == 2 * OH_J - 1))
                        if part == 1:
                            mm.then_inc(onehot_used if j < OH_J - 1 else product_done, 1)
                elif kind == "turn":
                    g = step[2]
                    bank = turn_bank_free(step)
                    pe.wait_ge(gathered[t][g], 16 * len(GROUPS[g]))
                    for i, m in enumerate(GROUPS[g]):
                        last = nc.tensor.transpose(turn[:, bank, i * P:(i + 1) * P], emb[:, t % EMB_BUFS, m, :],
                                                   ident[:, :])
                    last.then_inc(turned, 1)
                elif kind == "gram":
                    c = step[2]
                    if c == 0:
                        for step_before in list(turn_count)[groups_until(t) - 2:groups_until(t)]:
                            turn_result_read(step_before)
                    if t == 0 and c == 0:
                        pe.wait_ge(pad_zero, 1)
                        pe.wait_ge(product_out, NH)
                    if c == 0 and t >= 2:
                        pe.wait_ge(z_all_ready, t - 1)
                    for i in range(PER_BANK):
                        for s in range(QUADS):
                            b = t * P + (c * PER_BANK + i) * QUADS + s
                            last = nc.tensor.matmul(gps[QUAD * s:QUAD * (s + 1), t % 2, c, i * QUAD:(i + 1) * QUAD],
                                                    feat[:, b, :], feat[:, b, :], start=True, stop=True)
                    if c == HALVES - 1:
                        last.then_inc(gram_done, 1)
                elif kind == "base":
                    half = step[2]
                    if t == 0:
                        pe.wait_ge(w_in, 16 * WEIGHT_LOADS)
                        pe.wait_ge(ones_ready, 1)
                    elif t == TILES - 1:
                        pe.wait_ge(z_all_ready, t)
                    elif half == 0:
                        pe.wait_ge(h2_biased, t)
                    else:
                        pe.wait_ge(h1_dve, 2 * t)
                    if half == 0 and t == TILES - 1:
                        nc.tensor.matmul(mlp_bank(t, 1)[:, 2 * P:2 * P + H2], ones[:, :], b2[0:1, :], start=True,
                                         stop=False, skip_group_check=True)
                    for m in (2 * half, 2 * half + 1):
                        nc.tensor.matmul(mlp_bank(t, 1 - half)[:, m % 2 * P:(m % 2 + 1) * P],
                                         w1[:, ZCH, m * P:(m + 1) * P], bottom_t[:, t * P:(t + 1) * P],
                                         start=(m == (2 if t == TILES - 1 else 2 * half)), stop=False,
                                         skip_group_check=True)
                elif kind == "pairs":
                    bank = turn_bank_free(step)
                    pe.wait_ge(pairs_act, 2 * t + step[2] + 1)
                    if step[2] == 1:
                        pe.wait_ge(pairs_dve, t + 1)
                    for i, c in enumerate(PAIR_CHUNKS[step[2]]):
                        last = nc.tensor.transpose(turn[0:ZK, bank, i * P:(i + 1) * P],
                                                   pairs[:, c, :, :].rearrange("p i d -> p (i d)"), ident[:, :])
                    last.then_inc(z_turned, 1)
                elif kind == "layer1":
                    turn_result_read(("pairs", t, 0))
                    for part in range(len(PAIR_CHUNKS)):
                        if part == 1:
                            turn_result_read(("pairs", t, 1))
                        for m in (2 * step[2], 2 * step[2] + 1):
                            for c in PAIR_CHUNKS[part]:
                                last = nc.tensor.matmul(mlp_bank(t, 1 - m // 2)[:, m % 2 * P:(m % 2 + 1) * P],
                                                        w1[0:ZK, c, m * P:(m + 1) * P], z_t[0:ZK, c * P:(c + 1) * P],
                                                        start=False, stop=(c == ZCH - 1), skip_group_check=True)
                    last.then_inc(l1_done, 1)
                elif kind == "layer2":
                    pe.wait_ge(h1_act, t + 1)
                    for c in range(N1):
                        if c >= 2:
                            pe.wait_ge(h1_dve, 2 * t + c - 1)
                        last = nc.tensor.matmul(mlp_bank(t, 1)[:, 2 * P:2 * P + H2], h1[:, c, :], w2[:, c, :],
                                                start=(c == 0 and t < TILES - 1), stop=(c == N1 - 1),
                                                skip_group_check=True)
                    last.then_inc(l2_done, 1)


def pair_rows():
    rows = []
    for i in range(FEATS):
        for delta in range(1, DELTAS + 1):
            a, b = sorted((FEATURE_OF_SLOT[i], FEATURE_OF_SLOT[(i + delta) % FEATS]))
            rows.append(a * FEATS - a * (a + 1) // 2 + b - a - 1)
    return rows


def kernel(**inputs):
    import numpy as np
    import concourse.bacc as bacc
    from concourse.bass_utils import run_bass_kernel_spmd

    given = {name: np.asarray(a) for name, a in inputs.items()}
    w1 = given["W_top1"]
    sent = {name: given[name] for name in ["r_bottom_output", "ids", "W_top2"] + [f"tbl_{f}" for f in range(FIELDS)]}
    sent["ids_by_slot"] = given["ids"].T[ONEHOT]
    sent["W1_pairs"] = w1[pair_rows()]
    sent["W1_bottom"] = w1[PAIRS:]
    sent["b1_cols"] = given["b_top1"].reshape(N1, P).T
    sent["b2_row"] = given["b_top2"].reshape(1, H2)
    sent["W3_row"] = given["W_top3"].reshape(1, H2)

    nc = bacc.Bacc("TRN2", target_bir_lowering=False, num_devices=1)
    arrays, args = {}, {}
    for name, a in sent.items():
        a = np.ascontiguousarray(a)
        arrays[f"in_{name}_dram"] = a
        args[name] = nc.dram_tensor(f"in_{name}_dram", a.shape, mybir.dt.from_np(a.dtype), kind="ExternalInput").ap()
    out = nc.dram_tensor("out_0_dram", (B, 1), F32, kind="ExternalOutput").ap()
    dlrm_tower(nc, args, out)
    r = run_bass_kernel_spmd(nc, [arrays], core_ids=[0])
    return r.results[0]["out_0_dram"]
```
